# Optimizing a Trainium2 kernel written in Bass

```python
import numpy as np
import jax
import jax.numpy as jnp

def _softmax(x, axis=-1):
    return jax.nn.softmax(x, axis=axis)

def _gelu(x):
    return jax.nn.gelu(x, approximate=True)

def _silu(x):
    return jax.nn.silu(x)

def _sigmoid(x):
    return jax.nn.sigmoid(x)

def _layernorm(x, axis=-1, eps=1e-05):
    m = jnp.mean(x, axis=axis, keepdims=True)
    v = jnp.var(x, axis=axis, keepdims=True)
    return (x - m) / jnp.sqrt(v + eps)

def _scatter_add(tgt, idx, src, axis=0):
    return tgt.at[idx].add(src)

def _segment_sum(src, seg, n):
    return jax.ops.segment_sum(src, seg, n)
kernel_name = 'mk_adj_resnorm_d1_adj_r2_2edaef'

def setup_inputs(seed: int=0):
    np.random.seed(seed)
    _w = jnp.asarray

    def _rec_inputs():
        import jax
        import jax.numpy as jnp
        _gk = jax.random.key(seed)
        x = -0.0002422 + 1 * jax.random.normal(jax.random.fold_in(_gk, 1), (8, 1024, 512), jnp.float32)
        _a = jax.random.bernoulli(jax.random.fold_in(_gk, 2), 0.00195312, (8, 1024, 1024))
        adj = _a.astype(jnp.int32)
        return (x, adj)
    x, adj = _rec_inputs()

    def _L0_gnn_setup():
        import jax, jax.numpy as jnp
        import numpy as np
        IN_DIM = 512
        OUT_DIM = 512
        BATCH = 128
        NUM_OBJS = 100
        key = jax.random.key(seed)
        k1, k2, k3, k4, k5 = jax.random.split(key, 5)
        stdv = 1.0 / np.sqrt(OUT_DIM)
        feature = jax.random.normal(k1, (BATCH, NUM_OBJS, IN_DIM), dtype=jnp.float32)
        graph = jax.random.randint(k2, (BATCH, NUM_OBJS, NUM_OBJS), 0, 2, dtype=jnp.int32)
        weight = jax.random.uniform(k3, (IN_DIM, OUT_DIM), dtype=jnp.float32, minval=-stdv, maxval=stdv)
        wq = jax.random.uniform(k4, (IN_DIM, OUT_DIM), dtype=jnp.float32, minval=-stdv, maxval=stdv)
        wk = jax.random.uniform(k5, (IN_DIM, OUT_DIM), dtype=jnp.float32, minval=-stdv, maxval=stdv)
        return {'feature': feature, 'graph': graph, 'weight': weight, 'wq': wq, 'wk': wk}
    _L0_gnn_all = _L0_gnn_setup()
    _L0_gnn_in = {k: v for k, v in _L0_gnn_all.items() if k in ('weight', 'wq', 'wk')}
    del _L0_gnn_all
    return {'x': x, 'adj': adj, 'L0_gnn_weight': _L0_gnn_in['weight'], 'L0_gnn_wq': _L0_gnn_in['wq'], 'L0_gnn_wk': _L0_gnn_in['wk']}

def reference(x, adj, L0_gnn_weight, L0_gnn_wq, L0_gnn_wk):
    import jax
    import jax.numpy as jnp

    def _L0_gnn_ref(feature, graph, weight, wq, wk):
        import jax, jax.numpy as jnp
        import numpy as np
        IN_DIM = 512
        OUT_DIM = 512
        BATCH = 128
        NUM_OBJS = 100
        output = jnp.einsum('bni,io->bno', feature, weight)
        q = jnp.einsum('bni,io->bno', feature, wq)
        k = jnp.einsum('bni,io->bno', feature, wk)
        alpha = jnp.einsum('bno,bmo->bnm', q, k)
        alpha = jnp.maximum(alpha, 0.0) * (graph != 0).astype(alpha.dtype)
        alpha = jax.nn.softmax(alpha, axis=1)
        return jnp.einsum('bnm,bmo->bno', alpha, output)
    x = _layernorm(x + _L0_gnn_ref(x, adj, L0_gnn_weight, L0_gnn_wq, L0_gnn_wk), axis=-1)
    return x

_drawn_inputs = setup_inputs


def setup_inputs(seed=0):
    import zlib

    import numpy as np

    out = dict(_drawn_inputs(seed))
    spreads = {}
    factors = {}
    for name, (base, spread) in spreads.items():
        noise = np.random.default_rng([zlib.crc32(name.encode()), seed]).standard_normal(out[name].shape)
        drawn = base * np.exp(spread * noise) if base else spread * noise
        out[name] = jnp.asarray(drawn.astype(out[name].dtype))
    for name, factor in factors.items():
        out[name] = (out[name] * factor).astype(out[name].dtype)
    return out
```

```python
from contextlib import ExitStack

import concourse.bass as bass
from concourse import mybir

ALU = mybir.AluOpType
ACT = mybir.ActivationFunctionType
F32 = mybir.dt.float32
F32R = mybir.dt.float32r
I32 = mybir.dt.int32

P = 128
NFREE = 512
EPS = 1e-5


def graph_attention_layernorm(nc, x, x_t, adj_t, w, wq_t, wk_t, out):
    B, N, D = x.shape
    MT = N // P
    KT = D // P
    NH = N // NFREE
    QN = KT * NH
    XS = 4
    LATE = 6
    assert MT == 8 and D == NFREE and MT % XS == 0 and KT <= LATE

    with ExitStack() as ctx:
        def sb(name, shape, dt):
            return ctx.enter_context(nc.sbuf_tensor(name, shape, dt))

        def psum(name, shape, dt):
            return ctx.enter_context(nc.psum_tensor(name, shape, dt))

        def sem(name):
            return ctx.enter_context(nc.semaphore(name))

        xt_hi = sb("xt_hi", [P, KT, N], F32R)
        xt_lo = sb("xt_lo", [P, KT, N], F32R)
        q_hi = sb("q_hi", [P, KT, N], F32R)
        q_lo = sb("q_lo", [P, KT, N], F32R)
        v_hi = sb("v_hi", [P, MT, D], F32R)
        v_lo = sb("v_lo", [P, MT, D], F32R)
        a_hi = sb("a_hi", [P, KT, D], F32R)
        a_lo = sb("a_lo", [P, KT, D], F32R)
        w_hi = sb("w_hi", [P, KT, D], F32R)
        w_lo = sb("w_lo", [P, KT, D], F32R)
        p_hi = sb("p_hi", [P, 2, MT, P], F32R)
        p_lo = sb("p_lo", [P, 2, MT, P], F32R)
        probs = sb("probs", [P, MT, N], F32)
        xt_raw = sb("xt_raw", [P, 2, N], F32)
        graph = sb("graph", [P, 2, N], I32)
        rows = sb("rows", [P, XS, D], F32)
        least = sb("least", [P, MT], F32)
        total = sb("total", [P, MT], F32)
        inv_total = sb("inv_total", [P, MT], F32)
        stats = sb("stats", [P, 2, 6], F32)
        moments = sb("moments", [P, XS, 2], F32)
        var_eps = sb("var_eps", [P, XS], F32)
        rstd = sb("rstd", [P, XS], F32)
        shift = sb("shift", [P, XS], F32)
        eps = sb("eps", [P, 1], F32)
        minus_half = sb("minus_half", [P, 1], F32)

        score_ps = psum("score_ps", [P, 2, N], F32)
        proj_ps = psum("proj_ps", [P, 2, NFREE], F32)
        mix_ps = psum("mix_ps", [P, 2, D], F32)

        wq_loaded = sem("wq_loaded")
        wk_loaded = sem("wk_loaded")
        w_loaded = sem("w_loaded")
        xt_loaded = [sem(f"xt_loaded{i}") for i in range(2)]
        graph_loaded = [sem(f"graph_loaded{i}") for i in range(2)]
        rows_loaded = [sem(f"rows_loaded{i}") for i in range(XS)]
        rows_stored = [sem(f"rows_stored{i}") for i in range(XS)]
        weights_hi = sem("weights_hi")
        weights_lo = sem("weights_lo")
        a_done = sem("a_done")
        a_hi_done = sem("a_hi_done")
        a_split = sem("a_split")
        xt_hi_done = sem("xt_hi_done")
        xt_split = sem("xt_split")
        q_done = sem("q_done")
        q_hi_done = sem("q_hi_done")
        q_split = sem("q_split")
        scores_done = sem("scores_done")
        masked = sem("masked")
        clipped = sem("clipped")
        exp_done = sem("exp_done")
        inv_done = sem("inv_done")
        v_done = sem("v_done")
        v_hi_done = sem("v_hi_done")
        v_split = sem("v_split")
        p_hi_done = sem("p_hi_done")
        p_split = sem("p_split")
        mixed = sem("mixed")
        summed = sem("summed")
        stats_done = sem("stats_done")
        moments_done = sem("moments_done")
        constants = sem("constants")
        var_eps_done = sem("var_eps_done")
        rstd_done = sem("rstd_done")
        shift_done = sem("shift_done")
        normed = sem("normed")

        def staged(i):
            return probs[:, 2 * i:2 * i + 2, :].rearrange("p a (k e) -> p (a k) e", e=D)

        wq_hi, wk_hi = v_hi[:, 0:KT, :], v_hi[:, KT:2 * KT, :]
        wq_lo, wk_lo = v_lo[:, 0:KT, :], v_lo[:, KT:2 * KT, :]
        weight_parts = [(wq_hi, wq_lo), (wk_hi, wk_lo), (w_hi[:, :, :], w_lo[:, :, :])]
        weight_loaded = [wq_loaded, wk_loaded, w_loaded]

        block = ctx.enter_context(nc.Block())

        @block.sync
        def _(sp):
            def load_xt(b, k):
                sp.dma_start(xt_raw[:, k % 2, :], x_t[b, k * P:(k + 1) * P, :]).then_inc(xt_loaded[k % 2], 16)

            def load_graph(b, m):
                sp.dma_start(graph[:, m % 2, :], adj_t[b, m * P:(m + 1) * P, :]).then_inc(graph_loaded[m % 2], 16)

            def load_rows(b, n):
                sp.dma_start(rows[:, n % XS, :], x[b, n * P:(n + 1) * P, :]).then_inc(rows_loaded[n % XS], 16)

            def store_rows(b, n):
                sp.wait_ge(normed, b * MT + n + 1)
                sp.dma_start(out[b, n * P:(n + 1) * P, :], rows[:, n % XS, :]).then_inc(rows_stored[n % XS], 16)

            def batch(b):
                for m in range(2):
                    sp.wait_ge(masked, b * MT + MT - 1 + m)
                    load_graph(b + 1, m)
                for k in range(KT):
                    if k >= 2:
                        sp.wait_ge(xt_split, b * KT + KT + k - 1)
                    load_xt(b + 1, k)
                for n in range(MT):
                    store_rows(b, n)
                    if n + XS < MT:
                        sp.wait_ge(rows_stored[n % XS], b * (16 * MT // XS) + 16 * (n // XS + 1))
                        load_rows(b, n + XS)
                for m in range(2, MT):
                    sp.wait_ge(masked, b * MT + MT + m - 1)
                    load_graph(b + 1, m)
                for n in range(XS):
                    sp.wait_ge(rows_stored[n], b * (16 * MT // XS) + 16 * MT // XS)
                    load_rows(b + 1, n)

            for w_dram, i in ((wq_t, 0), (wk_t, 1)):
                sp.dma_start(staged(i), w_dram.rearrange("(k p) e -> p k e", p=P)).then_inc(weight_loaded[i], 16)
            load_xt(0, 0)
            load_xt(0, 1)
            for k in range(2, KT):
                sp.wait_ge(xt_split, k - 1)
                load_xt(0, k)
            sp.dma_start(staged(2), w.rearrange("(k p) e -> p k e", p=P)).then_inc(w_loaded, 16)
            for n in range(XS):
                load_rows(0, n)
            for m in range(MT):
                if m >= 2:
                    sp.wait_ge(masked, m - 1)
                load_graph(0, m)
            with sp.Fori(0, B - 1) as b:
                batch(b)
            for n in range(MT):
                store_rows(B - 1, n)
                if n + XS < MT:
                    sp.wait_ge(rows_stored[n % XS], (B - 1) * (16 * MT // XS) + 16 * (n // XS + 1))
                    load_rows(B - 1, n + XS)
            for s in range(XS):
                sp.wait_ge(rows_stored[s], 16 * B * MT // XS)

        @block.tensor
        def _(pe):
            def product(dst, left, right, ks, done):
                for k in ks:
                    hi, lo = left(k)
                    for i, d in enumerate(dst):
                        r_hi, r_lo = right(k, i)
                        pe.matmul(d, hi, r_hi, start=(k == ks[0]), stop=False)
                        pe.matmul(d, hi, r_lo, start=False, stop=False)
                    for i, d in enumerate(dst):
                        r_hi, _ = right(k, i)
                        mm = pe.matmul(d, lo, r_hi, start=False, stop=(k == ks[-1]))
                mm.then_inc(done, 1)

            def project_queries(b):
                pe.wait_ge(xt_split, b * KT + KT)
                for j in range(QN):
                    e, h = j // NH, j % NH
                    if j >= 2:
                        pe.wait_ge(q_split, b * QN + j - 1)
                    product([proj_ps[:, j % 2, :]],
                            lambda k: (a_hi[:, k, e * P:(e + 1) * P], a_lo[:, k, e * P:(e + 1) * P]),
                            lambda k, i: (xt_hi[:, k, h * NFREE:(h + 1) * NFREE],
                                          xt_lo[:, k, h * NFREE:(h + 1) * NFREE]),
                            range(KT), q_done)

            def mix(b, n):
                pe.wait_ge(p_split, b * MT + n + 1)
                if n >= 2:
                    pe.wait_ge(summed, b * MT + n - 1)
                for m in range(MT):
                    if n == 0:
                        pe.wait_ge(v_split, b * MT + m + 1)
                    hi, lo = p_hi[:, n % 2, m, :], p_lo[:, n % 2, m, :]
                    d = mix_ps[:, n % 2, :]
                    pe.matmul(d, hi, v_hi[:, m, :], start=(m == 0), stop=False)
                    pe.matmul(d, hi, v_lo[:, m, :], start=False, stop=False)
                    mm = pe.matmul(d, lo, v_hi[:, m, :], start=False, stop=(m == MT - 1))
                mm.then_inc(mixed, 1)

            def batch(b, last):
                pe.wait_ge(q_split, b * QN + QN)
                for m in range(MT):
                    if m >= 2:
                        pe.wait_ge(masked, b * MT + m - 1)
                    product([score_ps[:, m % 2, h * NFREE:(h + 1) * NFREE] for h in range(NH)],
                            lambda k: (xt_hi[:, k, m * P:(m + 1) * P], xt_lo[:, k, m * P:(m + 1) * P]),
                            lambda k, i: (q_hi[:, k, i * NFREE:(i + 1) * NFREE],
                                          q_lo[:, k, i * NFREE:(i + 1) * NFREE]),
                            range(KT), scores_done)
                for m in range(MT):
                    if m >= 2:
                        pe.wait_ge(v_split, b * MT + m - 1)
                    product([proj_ps[:, m % 2, :]],
                            lambda k: (xt_hi[:, k, m * P:(m + 1) * P], xt_lo[:, k, m * P:(m + 1) * P]),
                            lambda k, i: (w_hi[:, k, :], w_lo[:, k, :]),
                            range(KT), v_done)
                for n in range(LATE):
                    mix(b, n)
                if not last:
                    project_queries(b + 1)
                for n in range(LATE, MT):
                    mix(b, n)

            pe.wait_ge(weights_lo, 2)
            for t in range(KT):
                if t >= 2:
                    pe.wait_ge(a_split, t - 1)
                product([proj_ps[:, t % 2, :]],
                        lambda k: (wq_hi[:, k, t * P:(t + 1) * P], wq_lo[:, k, t * P:(t + 1) * P]),
                        lambda k, i: (wk_hi[:, k, :], wk_lo[:, k, :]),
                        range(KT), a_done)
            pe.wait_ge(a_split, KT)
            project_queries(0)
            pe.wait_ge(weights_lo, 3)
            with pe.Fori(0, B - 1) as b:
                batch(b, False)
            batch(B - 1, True)

        @block.scalar
        def _(act):
            def split_xt(b, k):
                act.wait_ge(xt_loaded[k % 2], b * (16 * KT // 2) + 16 * (k // 2 + 1))
                nc.scalar.copy(xt_hi[:, k, :], xt_raw[:, k % 2, :]).then_inc(xt_hi_done, 1)

            def split_q(b, j):
                act.wait_ge(q_done, b * QN + j + 1)
                e, h = j // NH, j % NH
                nc.scalar.copy(q_hi[:, e, h * NFREE:(h + 1) * NFREE], proj_ps[:, j % 2, :]).then_inc(q_hi_done, 1)

            def split_v(b, m):
                act.wait_ge(v_done, b * MT + m + 1)
                act.wait_ge(inv_done, b * MT + m + 1)
                nc.scalar.activation(v_hi[:, m, :], proj_ps[:, m % 2, :], ACT.Copy,
                                     scale=inv_total[:, m:m + 1]).then_inc(v_hi_done, 1)

            def split_p(b, n):
                if n == 0:
                    act.wait_ge(exp_done, b * MT + MT)
                if n >= 2:
                    act.wait_ge(mixed, b * MT + n - 1)
                nc.scalar.copy(p_hi[:, n % 2, :, :], probs[:, :, n * P:(n + 1) * P]).then_inc(p_hi_done, 1)

            def batch(b, last):
                for m in range(MT):
                    act.wait_ge(clipped, b * MT + m + 1)
                    nc.scalar.activation(probs[:, m, :], probs[:, m, :], ACT.Exp, bias=least[:, m:m + 1],
                                         scale=-1.0, accum_out=total[:, m:m + 1]).then_inc(exp_done, 1)
                for m in range(MT):
                    split_v(b, m)
                    if m == MT - 3:
                        split_p(b, 0)
                split_p(b, 1)
                for n in range(LATE):
                    split_p(b, n + 2)
                    if not last and n < KT:
                        if n == 0:
                            act.wait_ge(v_done, b * MT + MT)
                        split_xt(b + 1, n)
                if not last:
                    for j in range(QN):
                        split_q(b + 1, j)

            for i in range(2):
                act.wait_ge(weight_loaded[i], 16)
                nc.scalar.copy(weight_parts[i][0], staged(i)).then_inc(weights_hi, 1)
            for k in range(KT):
                split_xt(0, k)
            for t in range(KT):
                act.wait_ge(a_done, t + 1)
                nc.scalar.activation(a_hi[:, t, :], proj_ps[:, t % 2, :], ACT.Copy,
                                     scale=-1.0).then_inc(a_hi_done, 1)
            act.wait_ge(w_loaded, 16)
            nc.scalar.copy(weight_parts[2][0], staged(2)).then_inc(weights_hi, 1)
            for j in range(QN):
                split_q(0, j)
            with act.Fori(0, B - 1) as b:
                batch(b, False)
            batch(B - 1, True)

        @block.vector
        def _(dve):
            def split_xt(b, k):
                dve.wait_ge(xt_hi_done, b * KT + k + 1)
                nc.vector.tensor_tensor(xt_lo[:, k, :], xt_raw[:, k % 2, :], xt_hi[:, k, :].bitcast(F32),
                                        ALU.subtract).then_inc(xt_split, 1)

            def split_q(b, j):
                dve.wait_ge(q_hi_done, b * QN + j + 1)
                at = (slice(None), j // NH, slice((j % NH) * NFREE, (j % NH + 1) * NFREE))
                nc.vector.tensor_tensor(q_lo[at], proj_ps[:, j % 2, :], q_hi[at].bitcast(F32),
                                        ALU.subtract).then_inc(q_split, 1)

            def split_v(b, m):
                dve.wait_ge(v_hi_done, b * MT + m + 1)
                nc.vector.scalar_tensor_tensor(out=v_lo[:, m, :], in0=proj_ps[:, m % 2, :],
                                               scalar=inv_total[:, m:m + 1], in1=v_hi[:, m, :].bitcast(F32),
                                               op0=ALU.mult, op1=ALU.subtract).then_inc(v_split, 1)

            def split_p(b, n):
                dve.wait_ge(p_hi_done, b * MT + n + 1)
                nc.vector.tensor_tensor(p_lo[:, n % 2, :, :], probs[:, :, n * P:(n + 1) * P],
                                        p_hi[:, n % 2, :, :].bitcast(F32), ALU.subtract).then_inc(p_split, 1)

            def invert(b, m):
                dve.wait_ge(exp_done, b * MT + m + 1)
                nc.vector.reciprocal(inv_total[:, m:m + 1], total[:, m:m + 1]).then_inc(inv_done, 1)

            def finish(b, n):
                r = rows[:, n % XS, :]
                dve.wait_ge(mixed, b * MT + n + 1)
                dve.wait_ge(rows_loaded[n % XS], b * (16 * MT // XS) + 16 * (n // XS + 1))
                nc.vector.tensor_tensor(r, mix_ps[:, n % 2, :], r, ALU.add).then_inc(summed, 1)
                dve.wait_ge(summed, b * MT + n + 1)
                nc.vector.bn_stats(stats[:, n % 2, :], r).then_inc(stats_done, 1)
                dve.wait_ge(weights_lo, 3)
                dve.wait_ge(stats_done, b * MT + n + 1)
                nc.vector.bn_aggr(moments[:, n % XS, :], stats[:, n % 2, :]).then_inc(moments_done, 1)

            def batch(b, last):
                for m in range(MT):
                    s = probs[:, m, :]
                    dve.wait_ge(scores_done, b * MT + m + 1)
                    dve.wait_ge(graph_loaded[m % 2], b * (16 * MT // 2) + 16 * (m // 2 + 1))
                    nc.vector.scalar_tensor_tensor(out=s, in0=graph[:, m % 2, :], scalar=0.0,
                                                   in1=score_ps[:, m % 2, :], op0=ALU.not_equal,
                                                   op1=ALU.mult).then_inc(masked, 1)
                    dve.wait_ge(masked, b * MT + m + 1)
                    nc.vector.tensor_scalar(s, s, 0.0, None, ALU.min, ALU.min,
                                            accum_out=least[:, m:m + 1]).then_inc(clipped, 1)
                    if m >= 1:
                        invert(b, m - 1)
                invert(b, MT - 1)
                for m in range(MT):
                    split_v(b, m)
                    if m == MT - 3:
                        split_p(b, 0)
                split_p(b, 1)
                for n in range(LATE):
                    split_p(b, n + 2)
                    finish(b, n)
                    if not last and n < KT:
                        split_xt(b + 1, n)
                if not last:
                    for j in range(QN):
                        split_q(b + 1, j)
                for n in range(LATE, MT):
                    finish(b, n)

            for i in range(2):
                dve.wait_ge(weights_hi, i + 1)
                hi, lo = weight_parts[i]
                nc.vector.tensor_tensor(lo, staged(i), hi.bitcast(F32), ALU.subtract).then_inc(weights_lo, 1)
            for k in range(KT):
                split_xt(0, k)
            for t in range(KT):
                dve.wait_ge(a_hi_done, t + 1)
                nc.vector.scalar_tensor_tensor(out=a_lo[:, t, :], in0=proj_ps[:, t % 2, :], scalar=-1.0,
                                               in1=a_hi[:, t, :].bitcast(F32), op0=ALU.mult,
                                               op1=ALU.subtract).then_inc(a_split, 1)
            dve.wait_ge(weights_hi, 3)
            hi, lo = weight_parts[2]
            nc.vector.tensor_tensor(lo, staged(2), hi.bitcast(F32), ALU.subtract).then_inc(weights_lo, 1)
            for j in range(QN):
                split_q(0, j)
            dve.wait_ge(weights_lo, 3)
            with dve.Fori(0, B - 1) as b:
                batch(b, False)
            batch(B - 1, True)

        @block.gpsimd
        def _(pool):
            def normalise(b, n):
                s, r = n % XS, rows[:, n % XS, :]
                tiles = b * MT + n + 1
                pool.wait_ge(moments_done, tiles)
                nc.gpsimd.tensor_tensor(var_eps[:, s:s + 1], moments[:, s, 1:2], eps[:, :],
                                        ALU.add).then_inc(var_eps_done, 1)
                pool.wait_ge(var_eps_done, tiles)
                nc.gpsimd.tensor_tensor(rstd[:, s:s + 1], var_eps[:, s:s + 1], minus_half[:, :],
                                        ALU.pow).then_inc(rstd_done, 1)
                pool.wait_ge(constants, 2)
                pool.wait_ge(rstd_done, tiles)
                nc.gpsimd.tensor_scalar(shift[:, s:s + 1], moments[:, s, 0:1], -1.0, rstd[:, s:s + 1],
                                        ALU.mult, ALU.mult).then_inc(shift_done, 1)
                pool.wait_ge(constants, 2)
                pool.wait_ge(shift_done, tiles)
                nc.gpsimd.tensor_scalar(r, r, rstd[:, s:s + 1], shift[:, s:s + 1],
                                        ALU.mult, ALU.add).then_inc(normed, 1)

            nc.gpsimd.memset(eps[:, :], EPS).then_inc(constants, 1)
            nc.gpsimd.memset(minus_half[:, :], -0.5).then_inc(constants, 1)
            pool.wait_ge(constants, 2)
            with pool.Fori(0, B) as b:
                for n in range(MT):
                    normalise(b, n)


def kernel(x, adj, L0_gnn_weight, L0_gnn_wq, L0_gnn_wk):
    import numpy as _np
    import concourse.bacc as _bacc
    from concourse import mybir as _mybir
    from concourse.bass_utils import run_bass_kernel_spmd as _run

    x, adj = _np.asarray(x), _np.asarray(adj)
    arrays = {
        "x": _np.ascontiguousarray(x),
        "x_t": _np.ascontiguousarray(x.transpose(0, 2, 1)),
        "adj_t": _np.ascontiguousarray(adj.transpose(0, 2, 1)),
        "w": _np.ascontiguousarray(L0_gnn_weight),
        "wq_t": _np.ascontiguousarray(_np.asarray(L0_gnn_wq).T),
        "wk_t": _np.ascontiguousarray(_np.asarray(L0_gnn_wk).T),
    }
    nc = _bacc.Bacc("TRN2", target_bir_lowering=False, num_devices=1)
    args = [nc.dram_tensor(f"in_{name}", a.shape, _mybir.dt.from_np(a.dtype), kind="ExternalInput").ap()
            for name, a in arrays.items()]
    out = nc.dram_tensor("out", x.shape, _mybir.dt.float32, kind="ExternalOutput").ap()
    graph_attention_layernorm(nc, *args, out)
    r = _run(nc, [{f"in_{name}": a for name, a in arrays.items()}], core_ids=[0])
    return r.results[0]["out"]
```

```python
from contextlib import ExitStack

import concourse.bass as bass
from concourse import mybir

ALU = mybir.AluOpType
ACT = mybir.ActivationFunctionType
F32 = mybir.dt.float32
F32R = mybir.dt.float32r
I32 = mybir.dt.int32

P = 128
NFREE = 512
EPS = 1e-5


def graph_attention_layernorm(nc, x, x_t, adj_t, w, wq_t, wk_t, out):
    B, N, D = x.shape
    MT = N // P
    KT = D // P
    NH = N // NFREE
    QN = KT * NH
    XS = 4
    LATE = 6
    assert MT == 8 and D == NFREE and MT % XS == 0 and KT <= LATE

    with ExitStack() as ctx:
        def sb(name, shape, dt):
            return ctx.enter_context(nc.sbuf_tensor(name, shape, dt))

        def psum(name, shape, dt):
            return ctx.enter_context(nc.psum_tensor(name, shape, dt))

        def sem(name):
            return ctx.enter_context(nc.semaphore(name))

        xt_hi = sb("xt_hi", [P, KT, N], F32R)
        xt_lo = sb("xt_lo", [P, KT, N], F32R)
        q_hi = sb("q_hi", [P, KT, N], F32R)
        q_lo = sb("q_lo", [P, KT, N], F32R)
        v_hi = sb("v_hi", [P, MT, D], F32R)
        v_lo = sb("v_lo", [P, MT, D], F32R)
        a_hi = sb("a_hi", [P, KT, D], F32R)
        a_lo = sb("a_lo", [P, KT, D], F32R)
        w_hi = sb("w_hi", [P, KT, D], F32R)
        w_lo = sb("w_lo", [P, KT, D], F32R)
        p_hi = sb("p_hi", [P, 2, MT, P], F32R)
        p_lo = sb("p_lo", [P, 2, MT, P], F32R)
        probs = sb("probs", [P, MT, N], F32)
        xt_raw = sb("xt_raw", [P, 2, N], F32)
        graph = sb("graph", [P, 2, N], I32)
        rows = sb("rows", [P, XS, D], F32)
        least = sb("least", [P, MT], F32)
        total = sb("total", [P, MT], F32)
        inv_total = sb("inv_total", [P, MT], F32)
        stats = sb("stats", [P, 2, 6], F32)
        moments = sb("moments", [P, XS, 2], F32)
        var_eps = sb("var_eps", [P, XS], F32)
        rstd = sb("rstd", [P, XS], F32)
        shift = sb("shift", [P, XS], F32)
        eps = sb("eps", [P, 1], F32)
        minus_half = sb("minus_half", [P, 1], F32)

        score_ps = psum("score_ps", [P, 2, N], F32)
        proj_ps = psum("proj_ps", [P, 2, NFREE], F32)
        mix_ps = psum("mix_ps", [P, 2, D], F32)

        wqk_loaded = [sem(f"wqk_loaded{k}") for k in range(KT)]
        w_loaded = sem("w_loaded")
        xt_loaded = [sem(f"xt_loaded{i}") for i in range(2)]
        graph_loaded = [sem(f"graph_loaded{i}") for i in range(2)]
        rows_loaded = [sem(f"rows_loaded{i}") for i in range(XS)]
        rows_stored = [sem(f"rows_stored{i}") for i in range(XS)]
        wqk_hi_done = sem("wqk_hi_done")
        wqk_split = sem("wqk_split")
        w_hi_done = sem("w_hi_done")
        w_split = sem("w_split")
        a_done = sem("a_done")
        a_hi_done = sem("a_hi_done")
        a_split = sem("a_split")
        xt_hi_done = sem("xt_hi_done")
        xt_split = sem("xt_split")
        q_done = sem("q_done")
        q_hi_done = sem("q_hi_done")
        q_split = sem("q_split")
        scores_done = sem("scores_done")
        masked = sem("masked")
        clipped = sem("clipped")
        exp_done = sem("exp_done")
        inv_done = sem("inv_done")
        v_done = sem("v_done")
        v_hi_done = sem("v_hi_done")
        v_split = sem("v_split")
        p_hi_done = sem("p_hi_done")
        p_split = sem("p_split")
        mixed = sem("mixed")
        summed = sem("summed")
        stats_done = sem("stats_done")
        moments_done = sem("moments_done")
        constants = sem("constants")
        var_eps_done = sem("var_eps_done")
        rstd_done = sem("rstd_done")
        shift_done = sem("shift_done")
        normed = sem("normed")

        wqk_raw = probs[:, 0:KT, :].rearrange("p k (i e) -> p (k i) e", e=D)
        w_raw = probs[:, KT:KT + 2, :].rearrange("p a (k e) -> p (a k) e", e=D)
        a_ps = [proj_ps[:, 0, :], proj_ps[:, 1, :], mix_ps[:, 0, :], mix_ps[:, 1, :]]

        block = ctx.enter_context(nc.Block())

        @block.sync
        def _(sp):
            def load_xt(b, k):
                sp.dma_start(xt_raw[:, k % 2, :], x_t[b, k * P:(k + 1) * P, :]).then_inc(xt_loaded[k % 2], 16)

            def load_graph(b, m):
                sp.dma_start(graph[:, m % 2, :], adj_t[b, m * P:(m + 1) * P, :]).then_inc(graph_loaded[m % 2], 16)

            def load_rows(b, n):
                sp.dma_start(rows[:, n % XS, :], x[b, n * P:(n + 1) * P, :]).then_inc(rows_loaded[n % XS], 16)

            def store_rows(b, n):
                sp.wait_ge(normed, b * MT + n + 1)
                sp.dma_start(out[b, n * P:(n + 1) * P, :], rows[:, n % XS, :]).then_inc(rows_stored[n % XS], 16)

            def batch(b):
                for m in range(2):
                    sp.wait_ge(masked, b * MT + MT - 1 + m)
                    load_graph(b + 1, m)
                for k in range(KT):
                    if k >= 2:
                        sp.wait_ge(xt_split, b * KT + KT + k - 1)
                    load_xt(b + 1, k)
                for n in range(MT):
                    store_rows(b, n)
                    if n + XS < MT:
                        sp.wait_ge(rows_stored[n % XS], b * (16 * MT // XS) + 16 * (n // XS + 1))
                        load_rows(b, n + XS)
                for m in range(2, MT):
                    sp.wait_ge(masked, b * MT + MT + m - 1)
                    load_graph(b + 1, m)
                for n in range(XS):
                    sp.wait_ge(rows_stored[n], b * (16 * MT // XS) + 16 * MT // XS)
                    load_rows(b + 1, n)

            for k in range(KT):
                sp.dma_start(wqk_raw[:, 2 * k, :], wq_t[k * P:(k + 1) * P, :]).then_inc(wqk_loaded[k], 16)
            load_xt(0, 0)
            load_xt(0, 1)
            for k in range(2, KT):
                sp.wait_ge(xt_split, k - 1)
                load_xt(0, k)
            sp.dma_start(w_raw, w.rearrange("(k p) e -> p k e", p=P)).then_inc(w_loaded, 16)
            for n in range(XS):
                load_rows(0, n)
            for m in range(MT):
                if m >= 2:
                    sp.wait_ge(masked, m - 1)
                load_graph(0, m)
            with sp.Fori(0, B - 1) as b:
                batch(b)
            for n in range(MT):
                store_rows(B - 1, n)
                if n + XS < MT:
                    sp.wait_ge(rows_stored[n % XS], (B - 1) * (16 * MT // XS) + 16 * (n // XS + 1))
                    load_rows(B - 1, n + XS)
            for s in range(XS):
                sp.wait_ge(rows_stored[s], 16 * B * MT // XS)

        @block.tensor
        def _(pe):
            def product(dst, left, right, ks, done, parts=None, count=None):
                for k in ks:
                    if parts is not None:
                        pe.wait_ge(parts, count(k))
                    hi, lo = left(k)
                    for i, d in enumerate(dst):
                        r_hi, r_lo = right(k, i)
                        pe.matmul(d, hi, r_hi, start=(k == ks[0]), stop=False)
                        pe.matmul(d, hi, r_lo, start=False, stop=False)
                    for i, d in enumerate(dst):
                        r_hi, _ = right(k, i)
                        mm = pe.matmul(d, lo, r_hi, start=False, stop=(k == ks[-1]))
                mm.then_inc(done, 1)

            def project_queries(b, gate=()):
                pe.wait_ge(xt_split, b * KT + KT)
                for j in range(QN):
                    e, h = j // NH, j % NH
                    if j >= 2:
                        pe.wait_ge(q_split, b * QN + j - 1)
                    product([proj_ps[:, j % 2, :]],
                            lambda k: (a_hi[:, k, e * P:(e + 1) * P], a_lo[:, k, e * P:(e + 1) * P]),
                            lambda k, i: (xt_hi[:, k, h * NFREE:(h + 1) * NFREE],
                                          xt_lo[:, k, h * NFREE:(h + 1) * NFREE]),
                            range(KT), q_done, *(gate if j == 0 else ()))

            def mix(b, n):
                pe.wait_ge(p_split, b * MT + n + 1)
                if n >= 2:
                    pe.wait_ge(summed, b * MT + n - 1)
                for m in range(MT):
                    if n == 0:
                        pe.wait_ge(v_split, b * MT + m + 1)
                    hi, lo = p_hi[:, n % 2, m, :], p_lo[:, n % 2, m, :]
                    d = mix_ps[:, n % 2, :]
                    pe.matmul(d, hi, v_hi[:, m, :], start=(m == 0), stop=False)
                    pe.matmul(d, hi, v_lo[:, m, :], start=False, stop=False)
                    mm = pe.matmul(d, lo, v_hi[:, m, :], start=False, stop=(m == MT - 1))
                mm.then_inc(mixed, 1)

            def batch(b, last):
                for m in range(MT):
                    gate = (q_split, lambda k: b * QN + NH * (k + 1)) if m == 0 else ()
                    if m >= 2:
                        pe.wait_ge(masked, b * MT + m - 1)
                    product([score_ps[:, m % 2, h * NFREE:(h + 1) * NFREE] for h in range(NH)],
                            lambda k: (xt_hi[:, k, m * P:(m + 1) * P], xt_lo[:, k, m * P:(m + 1) * P]),
                            lambda k, i: (q_hi[:, k, i * NFREE:(i + 1) * NFREE],
                                          q_lo[:, k, i * NFREE:(i + 1) * NFREE]),
                            range(KT), scores_done, *gate)
                for m in range(MT):
                    if m >= 2:
                        pe.wait_ge(v_split, b * MT + m - 1)
                    product([proj_ps[:, m % 2, :]],
                            lambda k: (xt_hi[:, k, m * P:(m + 1) * P], xt_lo[:, k, m * P:(m + 1) * P]),
                            lambda k, i: (w_hi[:, k, :], w_lo[:, k, :]),
                            range(KT), v_done)
                for n in range(LATE):
                    mix(b, n)
                if not last:
                    project_queries(b + 1)
                for n in range(LATE, MT):
                    mix(b, n)

            for k in range(KT):
                pe.wait_ge(wqk_split, 2 * k + 2)
                for t in range(KT):
                    at, to = slice(t * P, (t + 1) * P), a_ps[t]
                    pe.matmul(to, v_hi[:, 2 * k, at], v_hi[:, 2 * k + 1, :], start=(k == 0), stop=False)
                    pe.matmul(to, v_hi[:, 2 * k, at], v_lo[:, 2 * k + 1, :], start=False, stop=False)
                    mm = pe.matmul(to, v_lo[:, 2 * k, at], v_hi[:, 2 * k + 1, :], start=False, stop=(k == KT - 1))
                    if k == KT - 1:
                        mm.then_inc(a_done, 1)
            project_queries(0, (a_split, lambda k: k + 1))
            pe.wait_ge(w_split, 1)
            with pe.Fori(0, B - 1) as b:
                batch(b, False)
            batch(B - 1, True)

        @block.scalar
        def _(act):
            def split_xt(b, k):
                act.wait_ge(xt_loaded[k % 2], b * (16 * KT // 2) + 16 * (k // 2 + 1))
                nc.scalar.copy(xt_hi[:, k, :], xt_raw[:, k % 2, :]).then_inc(xt_hi_done, 1)

            def split_q(b, j):
                act.wait_ge(q_done, b * QN + j + 1)
                e, h = j // NH, j % NH
                nc.scalar.copy(q_hi[:, e, h * NFREE:(h + 1) * NFREE], proj_ps[:, j % 2, :]).then_inc(q_hi_done, 1)

            def split_v(b, m):
                act.wait_ge(v_done, b * MT + m + 1)
                act.wait_ge(inv_done, b * MT + m + 1)
                nc.scalar.activation(v_hi[:, m, :], proj_ps[:, m % 2, :], ACT.Copy,
                                     scale=inv_total[:, m:m + 1]).then_inc(v_hi_done, 1)

            def split_p(b, n):
                if n == 0:
                    act.wait_ge(exp_done, b * MT + MT)
                if n >= 2:
                    act.wait_ge(mixed, b * MT + n - 1)
                nc.scalar.copy(p_hi[:, n % 2, :, :], probs[:, :, n * P:(n + 1) * P]).then_inc(p_hi_done, 1)

            def batch(b, last):
                for m in range(MT):
                    act.wait_ge(clipped, b * MT + m + 1)
                    nc.scalar.activation(probs[:, m, :], probs[:, m, :], ACT.Exp, bias=least[:, m:m + 1],
                                         scale=-1.0, accum_out=total[:, m:m + 1]).then_inc(exp_done, 1)
                for m in range(MT):
                    split_v(b, m)
                    if m == MT - 3:
                        split_p(b, 0)
                split_p(b, 1)
                for n in range(LATE):
                    split_p(b, n + 2)
                    if not last and n < KT:
                        if n == 0:
                            act.wait_ge(v_done, b * MT + MT)
                        split_xt(b + 1, n)
                if not last:
                    for j in range(QN):
                        split_q(b + 1, j)

            for k in range(KT):
                act.dma_start(wqk_raw[:, 2 * k + 1, :], wk_t[k * P:(k + 1) * P, :]).then_inc(wqk_loaded[k], 16)
            for i in range(2 * KT):
                act.wait_ge(wqk_loaded[i // 2], 32)
                nc.scalar.copy(v_hi[:, i, :], wqk_raw[:, i, :]).then_inc(wqk_hi_done, 1)
            for k in range(KT):
                split_xt(0, k)
            for t in range(KT):
                act.wait_ge(a_done, t + 1)
                nc.scalar.activation(a_hi[:, t, :], a_ps[t], ACT.Copy, scale=-1.0).then_inc(a_hi_done, 1)
            act.wait_ge(w_loaded, 16)
            nc.scalar.copy(w_hi[:, :, :], w_raw).then_inc(w_hi_done, 1)
            for j in range(QN):
                split_q(0, j)
            with act.Fori(0, B - 1) as b:
                batch(b, False)
            batch(B - 1, True)

        @block.vector
        def _(dve):
            def split_xt(b, k):
                dve.wait_ge(xt_hi_done, b * KT + k + 1)
                nc.vector.tensor_tensor(xt_lo[:, k, :], xt_raw[:, k % 2, :], xt_hi[:, k, :].bitcast(F32),
                                        ALU.subtract).then_inc(xt_split, 1)

            def split_q(b, j):
                dve.wait_ge(q_hi_done, b * QN + j + 1)
                at = (slice(None), j // NH, slice((j % NH) * NFREE, (j % NH + 1) * NFREE))
                nc.vector.tensor_tensor(q_lo[at], proj_ps[:, j % 2, :], q_hi[at].bitcast(F32),
                                        ALU.subtract).then_inc(q_split, 1)

            def split_v(b, m):
                dve.wait_ge(v_hi_done, b * MT + m + 1)
                nc.vector.scalar_tensor_tensor(out=v_lo[:, m, :], in0=proj_ps[:, m % 2, :],
                                               scalar=inv_total[:, m:m + 1], in1=v_hi[:, m, :].bitcast(F32),
                                               op0=ALU.mult, op1=ALU.subtract).then_inc(v_split, 1)

            def split_p(b, n):
                dve.wait_ge(p_hi_done, b * MT + n + 1)
                nc.vector.tensor_tensor(p_lo[:, n % 2, :, :], probs[:, :, n * P:(n + 1) * P],
                                        p_hi[:, n % 2, :, :].bitcast(F32), ALU.subtract).then_inc(p_split, 1)

            def invert(b, m):
                dve.wait_ge(exp_done, b * MT + m + 1)
                nc.vector.reciprocal(inv_total[:, m:m + 1], total[:, m:m + 1]).then_inc(inv_done, 1)

            def finish(b, n):
                r = rows[:, n % XS, :]
                dve.wait_ge(mixed, b * MT + n + 1)
                dve.wait_ge(rows_loaded[n % XS], b * (16 * MT // XS) + 16 * (n // XS + 1))
                nc.vector.tensor_tensor(r, mix_ps[:, n % 2, :], r, ALU.add).then_inc(summed, 1)
                dve.wait_ge(summed, b * MT + n + 1)
                nc.vector.bn_stats(stats[:, n % 2, :], r).then_inc(stats_done, 1)
                dve.wait_ge(w_split, 1)
                dve.wait_ge(stats_done, b * MT + n + 1)
                nc.vector.bn_aggr(moments[:, n % XS, :], stats[:, n % 2, :]).then_inc(moments_done, 1)

            def batch(b, last):
                for m in range(MT):
                    s = probs[:, m, :]
                    dve.wait_ge(scores_done, b * MT + m + 1)
                    dve.wait_ge(graph_loaded[m % 2], b * (16 * MT // 2) + 16 * (m // 2 + 1))
                    nc.vector.scalar_tensor_tensor(out=s, in0=graph[:, m % 2, :], scalar=0.0,
                                                   in1=score_ps[:, m % 2, :], op0=ALU.not_equal,
                                                   op1=ALU.mult).then_inc(masked, 1)
                    dve.wait_ge(masked, b * MT + m + 1)
                    nc.vector.tensor_scalar(s, s, 0.0, None, ALU.min, ALU.min,
                                            accum_out=least[:, m:m + 1]).then_inc(clipped, 1)
                    if m >= 1:
                        invert(b, m - 1)
                invert(b, MT - 1)
                for m in range(MT):
                    split_v(b, m)
                    if m == MT - 3:
                        split_p(b, 0)
                split_p(b, 1)
                for n in range(LATE):
                    split_p(b, n + 2)
                    finish(b, n)
                    if not last and n < KT:
                        split_xt(b + 1, n)
                if not last:
                    for j in range(QN):
                        split_q(b + 1, j)
                for n in range(LATE, MT):
                    finish(b, n)

            for i in range(2 * KT):
                dve.wait_ge(wqk_hi_done, i + 1)
                nc.vector.tensor_tensor(v_lo[:, i, :], wqk_raw[:, i, :], v_hi[:, i, :].bitcast(F32),
                                        ALU.subtract).then_inc(wqk_split, 1)
            for k in range(KT):
                split_xt(0, k)
            for t in range(KT):
                dve.wait_ge(a_hi_done, t + 1)
                nc.vector.scalar_tensor_tensor(out=a_lo[:, t, :], in0=a_ps[t], scalar=-1.0,
                                               in1=a_hi[:, t, :].bitcast(F32), op0=ALU.mult,
                                               op1=ALU.subtract).then_inc(a_split, 1)
            dve.wait_ge(w_hi_done, 1)
            nc.vector.tensor_tensor(w_lo[:, :, :], w_raw, w_hi[:, :, :].bitcast(F32),
                                    ALU.subtract).then_inc(w_split, 1)
            for j in range(QN):
                split_q(0, j)
            dve.wait_ge(w_split, 1)
            with dve.Fori(0, B - 1) as b:
                batch(b, False)
            batch(B - 1, True)

        @block.gpsimd
        def _(pool):
            def normalise(b, n):
                s, r = n % XS, rows[:, n % XS, :]
                tiles = b * MT + n + 1
                pool.wait_ge(moments_done, tiles)
                nc.gpsimd.tensor_tensor(var_eps[:, s:s + 1], moments[:, s, 1:2], eps[:, :],
                                        ALU.add).then_inc(var_eps_done, 1)
                pool.wait_ge(var_eps_done, tiles)
                nc.gpsimd.tensor_tensor(rstd[:, s:s + 1], var_eps[:, s:s + 1], minus_half[:, :],
                                        ALU.pow).then_inc(rstd_done, 1)
                pool.wait_ge(constants, 2)
                pool.wait_ge(rstd_done, tiles)
                nc.gpsimd.tensor_scalar(shift[:, s:s + 1], moments[:, s, 0:1], -1.0, rstd[:, s:s + 1],
                                        ALU.mult, ALU.mult).then_inc(shift_done, 1)
                pool.wait_ge(constants, 2)
                pool.wait_ge(shift_done, tiles)
                nc.gpsimd.tensor_scalar(r, r, rstd[:, s:s + 1], shift[:, s:s + 1],
                                        ALU.mult, ALU.add).then_inc(normed, 1)

            nc.gpsimd.memset(eps[:, :], EPS).then_inc(constants, 1)
            nc.gpsimd.memset(minus_half[:, :], -0.5).then_inc(constants, 1)
            pool.wait_ge(constants, 2)
            with pool.Fori(0, B) as b:
                for n in range(MT):
                    normalise(b, n)


def kernel(x, adj, L0_gnn_weight, L0_gnn_wq, L0_gnn_wk):
    import numpy as _np
    import concourse.bacc as _bacc
    from concourse import mybir as _mybir
    from concourse.bass_utils import run_bass_kernel_spmd as _run

    x, adj = _np.asarray(x), _np.asarray(adj)
    arrays = {
        "x": _np.ascontiguousarray(x),
        "x_t": _np.ascontiguousarray(x.transpose(0, 2, 1)),
        "adj_t": _np.ascontiguousarray(adj.transpose(0, 2, 1)),
        "w": _np.ascontiguousarray(L0_gnn_weight),
        "wq_t": _np.ascontiguousarray(_np.asarray(L0_gnn_wq).T),
        "wk_t": _np.ascontiguousarray(_np.asarray(L0_gnn_wk).T),
    }
    nc = _bacc.Bacc("TRN2", target_bir_lowering=False, num_devices=1)
    args = [nc.dram_tensor(f"in_{name}", a.shape, _mybir.dt.from_np(a.dtype), kind="ExternalInput").ap()
            for name, a in arrays.items()]
    out = nc.dram_tensor("out", x.shape, _mybir.dt.float32, kind="ExternalOutput").ap()
    graph_attention_layernorm(nc, *args, out)
    r = _run(nc, [{f"in_{name}": a for name, a in arrays.items()}], core_ids=[0])
    return r.results[0]["out"]
```
